# Optimizing a Trainium2 kernel written in Bass

```python
import numpy as np
import jax
import jax.numpy as jnp

def _softmax(x, axis=-1):
    return jax.nn.softmax(x, axis=axis)

def _gelu(x):
    return jax.nn.gelu(x, approximate=True)

def _silu(x):
    return jax.nn.silu(x)

def _sigmoid(x):
    return jax.nn.sigmoid(x)

def _layernorm(x, axis=-1, eps=1e-05):
    m = jnp.mean(x, axis=axis, keepdims=True)
    v = jnp.var(x, axis=axis, keepdims=True)
    return (x - m) / jnp.sqrt(v + eps)

def _scatter_add(tgt, idx, src, axis=0):
    return tgt.at[idx].add(src)

def _segment_sum(src, seg, n):
    return jax.ops.segment_sum(src, seg, n)
kernel_name = 'mk_cond_resid_d2_seqx_r8_4d8286'

def setup_inputs(seed: int=0):
    np.random.seed(seed)
    _w = jnp.asarray

    def _rec_inputs():
        import jax
        import jax.numpy as jnp
        _rk = jax.random.key(seed)
        x = -0.000125 + 0.9999 * jax.random.normal(jax.random.fold_in(_rk, 1), (64, 32, 512), jnp.float32)
        _lenS = 32 - jax.random.randint(jax.random.fold_in(_rk, 7), (64,), 0, max(1, 32 // 4) + 1, jnp.int32)
        _lenS2 = 32 - jax.random.randint(jax.random.fold_in(_rk, 8), (64,), 0, max(1, 32 // 4) + 1, jnp.int32)
        itok_B_3_7 = jax.random.randint(jax.random.fold_in(_rk, 11), (64,), 3, 8, jnp.int32)
        itok_B_0_15 = jax.random.randint(jax.random.fold_in(_rk, 12), (64,), 0, 16, jnp.int32)
        return (x, itok_B_3_7, itok_B_0_15)
    x, itok_B_3_7, itok_B_0_15 = _rec_inputs()

    def _L0_cond_setup():
        import jax, jax.numpy as jnp
        import numpy as np
        MAX_LORAS, OUT, IN = (8, 512, 512)
        B, S = (4, 256)
        key = jax.random.key(seed)
        k1, k2, k3 = jax.random.split(key, 3)
        x = jax.random.normal(k1, (B, S, IN), dtype=jnp.float32)
        weight = jax.random.normal(k2, (MAX_LORAS, OUT, IN), dtype=jnp.float32) * 0.02
        adapter_ids = jax.random.randint(k3, (B,), 0, MAX_LORAS, dtype=jnp.int32)
        return {'x': x, 'weight': weight, 'adapter_ids': adapter_ids}
    _L0_cond_all = _L0_cond_setup()
    _L0_cond_in = {k: v for k, v in _L0_cond_all.items() if k in ('weight',)}
    del _L0_cond_all

    def _L1_cond_setup():
        import jax, jax.numpy as jnp
        import numpy as np
        B, C, T = (64, 32, 512)
        S, D = (16, 32)
        key = jax.random.key(seed)
        k1, k2, k3 = jax.random.split(key, 3)
        x = jax.random.normal(k1, (B, C, T), dtype=jnp.float32)
        condition = jax.random.randint(k2, (B,), 0, S, dtype=jnp.int64)
        bound = float(np.sqrt(6.0 / C))
        weights = jax.random.uniform(k3, (S, C, D), dtype=jnp.float32, minval=-bound, maxval=bound)
        return {'x': x, 'condition': condition, 'weights': weights}
    _L1_cond_all = _L1_cond_setup()
    _L1_cond_in = {k: v for k, v in _L1_cond_all.items() if k in ('weights',)}
    del _L1_cond_all
    return {'x': x, 'itok_B_3_7': itok_B_3_7, 'itok_B_0_15': itok_B_0_15, 'L0_cond_weight': _L0_cond_in['weight'], 'L1_cond_weights': _L1_cond_in['weights']}

def reference(x, itok_B_3_7, itok_B_0_15, L0_cond_weight, L1_cond_weights):
    import jax
    import jax.numpy as jnp

    def _L0_cond_ref(x, weight, adapter_ids):
        import jax, jax.numpy as jnp
        import numpy as np
        MAX_LORAS, OUT, IN = (8, 512, 512)
        B, S = (4, 256)
        w = weight[adapter_ids]
        return jnp.einsum('bsi,boi->bso', x, w)

    def _L1_cond_ref(x, condition, weights):
        import jax, jax.numpy as jnp
        import numpy as np
        B, C, T = (64, 32, 512)
        S, D = (16, 32)
        W = weights[condition]
        return jnp.einsum('bct,bcd->bdt', x, W)
    x = x + _L0_cond_ref(x, L0_cond_weight, itok_B_3_7)
    x = x + _L1_cond_ref(x, itok_B_0_15, L1_cond_weights)
    return x

_drawn_inputs = setup_inputs


def setup_inputs(seed=0):
    import zlib

    import numpy as np

    out = dict(_drawn_inputs(seed))
    spreads = {}
    factors = {}
    for name, (base, spread) in spreads.items():
        noise = np.random.default_rng([zlib.crc32(name.encode()), seed]).standard_normal(out[name].shape)
        drawn = base * np.exp(spread * noise) if base else spread * noise
        out[name] = jnp.asarray(drawn.astype(out[name].dtype))
    for name, factor in factors.items():
        out[name] = (out[name] * factor).astype(out[name].dtype)
    return out
```

```python
from contextlib import ExitStack

import concourse.bass as bass
import numpy as np
from concourse import mybir

F32 = mybir.dt.float32
F32R = mybir.dt.float32r
I32 = mybir.dt.int32
U32 = mybir.dt.uint32
ALU = mybir.AluOpType
AX = mybir.AxisListType

P = 128
BATCH, CH, STEPS = 64, 32, 512
ADAPTERS, CONDS = 8, 16
ROWS = BATCH * CH
SLOTS = P // CH
CHUNKS = STEPS // P
MIN_TILES = BATCH // SLOTS
MAX_TILES = (BATCH + ADAPTERS * (SLOTS - 1)) // SLOTS
PAIRS = MAX_TILES // 2
MIN_PAIRS = MIN_TILES // 2
LISTED = MAX_TILES + 2
RAW_BUFS = 4

C_IDENT = 0
C_CHMASK = C_IDENT + P
C_MASK = C_CHMASK + SLOTS
C_XROW = C_MASK + SLOTS
C_WROW = C_XROW + 1
C_BLOCK = C_WROW + 1
C_SLOT = C_BLOCK + CH
C_BATCH = C_SLOT + LISTED * SLOTS
C_BEFORE = C_BATCH + P
C_ONES = C_BEFORE + BATCH
C_END = C_ONES + P

M_USED = 0
M_N_USED = M_USED + ADAPTERS
M_N_PAIRS = M_N_USED + 1
M_PLACE = M_N_PAIRS + 1
M_END = M_PLACE + LISTED


def constants():
    c = np.zeros((P, C_END), np.float32)
    row = np.arange(P)
    c[:, C_IDENT:C_IDENT + P] = np.eye(P)
    slot = row[:, None] // CH == np.arange(SLOTS)
    c[:, C_CHMASK:C_CHMASK + SLOTS] = slot * CH
    c[:, C_MASK:C_MASK + SLOTS] = slot
    c[:, C_XROW] = ROWS + row % CH
    c[:, C_WROW] = row % CH
    c[:, C_BLOCK:C_BLOCK + CH] = row[:, None] % CH == np.arange(CH)
    c[:, C_SLOT:C_BATCH] = np.arange(LISTED * SLOTS)
    c[:, C_BATCH:C_BEFORE] = row[:, None] - BATCH
    c[:, C_BEFORE:C_ONES] = np.arange(BATCH) < row[:, None]
    c[:, C_ONES:C_END] = 1.0
    return c


def build(nc, x, ids, w0, w1, const, out):
    with ExitStack() as ctx:
        def sb(name, shape, dt=F32):
            return ctx.enter_context(nc.sbuf_tensor(name, shape, dt))

        def sem(name):
            return ctx.enter_context(nc.semaphore(name))

        w_raw = sb("w_raw", [P, RAW_BUFS, CHUNKS * STEPS])
        w_hi = sb("w_hi", [P, ADAPTERS, CHUNKS * STEPS], F32R)
        w_lo = sb("w_lo", [P, ADAPTERS, CHUNKS * STEPS], F32R)
        x_tile = sb("x_tile", [P, 2, STEPS])
        w1_rows = sb("w1_rows", [P, 2, CH])
        w1_eye = sb("w1_eye", [P, 2, CH])
        block = sb("block", [P, 2, P])
        u_hi = sb("u_hi", [P, 2, CHUNKS * P], F32R)
        u_lo = sb("u_lo", [P, 2, CHUNKS * P], F32R)
        z_tile = sb("z_tile", [P, 2, STEPS])
        cst = sb("cst", [P, C_END])
        idt = sb("idt", [BATCH, 2 + BATCH], I32)
        idf = sb("idf", [BATCH, 2])
        onehot = sb("onehot", [BATCH, ADAPTERS])
        same_before = sb("same_before", [BATCH, BATCH])
        rank = sb("rank", [BATCH, 1])
        id1_wide = sb("id1_wide", [BATCH, P])
        tiles_i = sb("tiles_i", [P, ADAPTERS], I32)
        tiles_s = sb("tiles_s", [P, ADAPTERS], I32)
        tiles = sb("tiles", [P, ADAPTERS])
        tiles_end = sb("tiles_end", [P, ADAPTERS])
        tiles_from = sb("tiles_from", [P, ADAPTERS])
        present = sb("present", [P, ADAPTERS])
        places_end = sb("places_end", [P, ADAPTERS])
        places = sb("places", [P, ADAPTERS])
        named = sb("named", [P, ADAPTERS])
        at_place = sb("at_place", [1, ADAPTERS, ADAPTERS])
        base_terms = sb("base_terms", [BATCH, ADAPTERS])
        base = sb("base", [BATCH, 1])
        in_slot = sb("in_slot", [BATCH, LISTED * SLOTS])
        picked = sb("picked", [P, 2 * LISTED, SLOTS])
        picked_sum = sb("picked_sum", [P, 2 * LISTED])
        x_index = sb("x_index", [P, LISTED], U32)
        w1_index = sb("w1_index", [P, LISTED], U32)
        last_tile = sb("last_tile", [1, 1])
        tile_no = sb("tile_no", [1, LISTED])
        ended = sb("ended", [1, LISTED, ADAPTERS])
        half_i = sb("half_i", [1, 1], I32)
        meta = sb("meta", [1, M_END], I32)

        counts_ps = ctx.enter_context(nc.psum_tensor("counts_ps", [P, ADAPTERS], F32))
        slots_ps = ctx.enter_context(nc.psum_tensor("slots_ps", [P, 2 * LISTED * SLOTS], F32))
        u_ps = [ctx.enter_context(nc.psum_tensor(f"u_ps{i}", [P, CHUNKS * P], F32)) for i in range(2)]
        z_ps = [ctx.enter_context(nc.psum_tensor(f"z_ps{i}", [P, STEPS], F32)) for i in range(2)]

        tables_landed = sem("tables_landed")
        raw_landed = [sem(f"raw_landed{i}") for i in range(RAW_BUFS)]
        x_landed = [sem(f"x_landed{i}") for i in range(2)]
        w1_landed = [sem(f"w1_landed{i}") for i in range(2)]
        rows_zeroed = sem("rows_zeroed")
        table_step = sem("table_step")
        onehot_ready = sem("onehot_ready")
        counts_ready = sem("counts_ready")
        in_slot_ready = sem("in_slot_ready")
        slots_ready = sem("slots_ready")
        used_ready = sem("used_ready")
        index_ready = sem("index_ready")
        meta_ready = sem("meta_ready")
        eye_added = sem("eye_added")
        w_hi_ready = sem("w_hi_ready")
        w_split = sem("w_split")
        w1_eye_ready = sem("w1_eye_ready")
        block_ready = sem("block_ready")
        u_ready = sem("u_ready")
        u_hi_ready = sem("u_hi_ready")
        u_split = sem("u_split")
        z_ready = sem("z_ready")
        z_copied = sem("z_copied")
        z_stored = [sem(f"z_stored{i}") for i in range(2)]

        def const_of(start, width, rows=P):
            return cst[0:rows, start:start + width]

        def entry(eng, at, largest, least=0):
            return eng.value_load(meta[0:1, at:at + 1] if isinstance(at, int) else meta[0:1, bass.ds(at, 1)],
                                  min_val=least, max_val=largest)

        def optional_pairs(eng, n_pairs, pair, last=None):
            def from_pair(i):
                if i == PAIRS:
                    if last:
                        last(i)
                    return
                with eng.If(n_pairs > i):
                    pair(i)
                    from_pair(i + 1)
                if last:
                    with eng.Else():
                        last(i)
            from_pair(MIN_PAIRS)

        SPLIT_PAIRS = (ADAPTERS - 2) // 2

        prog = ctx.enter_context(nc.Block())

        @prog.sync
        def _(sp):
            sp.dma_start(idt[:], ids).then_inc(tables_landed, 16)
            sp.dma_start(cst[:], const).then_inc(tables_landed, 16)
            sp.wait_ge(used_ready, 1)
            n_used = entry(sp, M_N_USED, ADAPTERS, 1)

            def load_from(k):
                with sp.If(n_used > k):
                    if k >= RAW_BUFS:
                        sp.wait_ge(w_split, k - RAW_BUFS + 1)
                    which = entry(sp, M_USED + k, ADAPTERS - 1)
                    sp.dma_start(w_raw[:, k % RAW_BUFS, :],
                                 w0[bass.ds(which, 1)].rearrange("a p n -> p (a n)")
                                 ).then_inc(raw_landed[k % RAW_BUFS], 16)
                    if k + 1 < ADAPTERS:
                        load_from(k + 1)
            load_from(0)

        @prog.gpsimd
        def _(pool):
            nc.gpsimd.memset(x_tile[:], 0.0).then_inc(rows_zeroed, 1)
            pool.wait_ge(rows_zeroed, 1)

            def gather(t):
                if t >= 2:
                    pool.wait_ge(u_ready, t - 1)
                nc.gpsimd.indirect_dma_start(
                    x_tile[:, t % 2, :], None, x,
                    bass.IndirectOffsetOnAxis(ap=x_index[:, t:t + 1], axis=0),
                    bounds_check=ROWS - 1, oob_is_err=False).then_inc(x_landed[t % 2], 16)
                if t >= 2:
                    pool.wait_ge(w1_eye_ready, t - 1)
                nc.gpsimd.indirect_dma_start(
                    w1_rows[:, t % 2, :], None, w1,
                    bass.IndirectOffsetOnAxis(ap=w1_index[:, t:t + 1], axis=0),
                    bounds_check=CONDS * CH - 1, oob_is_err=False).then_inc(w1_landed[t % 2], 16)

            def scatter(t):
                pool.wait_ge(z_copied, t + 1)
                nc.gpsimd.indirect_dma_start(
                    out, bass.IndirectOffsetOnAxis(ap=x_index[:, t:t + 1], axis=0),
                    z_tile[:, t % 2, :], None,
                    bounds_check=ROWS - 1, oob_is_err=False).then_inc(z_stored[t % 2], 16)

            def pair(i):
                for t in (2 * i, 2 * i + 1):
                    gather(t + 2)
                    if t >= 1:
                        scatter(t - 1)

            pool.wait_ge(index_ready, 1)
            gather(0)
            gather(1)
            for i in range(MIN_PAIRS):
                pair(i)
            pool.wait_ge(meta_ready, 1)
            n_pairs = entry(pool, M_N_PAIRS, PAIRS, MIN_PAIRS)
            def last(i):
                scatter(2 * i - 1)
                for parity in range(2):
                    pool.wait_ge(z_stored[parity], 16 * i)
                    pool.wait_ge(x_landed[parity], 16 * (i + 1))
                    pool.wait_ge(w1_landed[parity], 16 * (i + 1))

            optional_pairs(pool, n_pairs, pair, last)

        @prog.scalar
        def _(act):
            def weight_hi(k):
                act.wait_ge(eye_added, k + 1)
                nc.scalar.copy(w_hi[:, k, :], w_raw[:, k % RAW_BUFS, :]).then_inc(w_hi_ready, 1)

            def u_high(t, parity):
                act.wait_ge(u_ready, t + 1)
                nc.scalar.copy(u_hi[:, parity, :], u_ps[parity][:]).then_inc(u_hi_ready, 1)

            def z_out(t, parity):
                act.wait_ge(z_ready, t + 1)
                uses = (t - parity) // 2 if isinstance(t, int) else (t - parity) * 8
                if isinstance(t, int):
                    if t >= 2:
                        act.wait_ge(z_stored[parity], 16 * uses)
                else:
                    act.wait_ge(z_stored[parity], uses)
                nc.scalar.copy(z_tile[:, parity, :], z_ps[parity][:]).then_inc(z_copied, 1)

            def half(t, parity, k=None):
                if not isinstance(t, int) or t >= 1:
                    z_out(t - 1, 1 - parity)
                u_high(t + 1, 1 - parity)
                if k is not None:
                    with act.If(n_used > k):
                        weight_hi(k)

            def pair(i, k=None):
                half(2 * i, 0, k)
                half(2 * i + 1, 1, None if k is None else k + 1)

            weight_hi(0)
            act.wait_ge(meta_ready, 1)
            n_used = entry(act, M_N_USED, ADAPTERS, 1)
            n_pairs = entry(act, M_N_PAIRS, PAIRS, MIN_PAIRS)
            u_high(0, 0)
            with act.If(n_used > 1):
                weight_hi(1)
            for i in range(SPLIT_PAIRS):
                pair(i, 2 * i + 2)
            with act.Fori(SPLIT_PAIRS, MIN_PAIRS) as i:
                pair(i)
            optional_pairs(act, n_pairs, pair, lambda pairs: z_out(2 * pairs - 1, 1))

        @prog.vector
        def _(dve):
            steps = [0]

            def link(ins):
                steps[0] += 1
                ins.then_inc(table_step, 1)
                dve.wait_ge(table_step, steps[0])

            v = nc.vector
            dve.wait_ge(tables_landed, 32)
            link(v.tensor_copy(idf[:], idt[:, 0:2]))
            v.tensor_scalar(onehot[:], const_of(C_SLOT, ADAPTERS, BATCH), idf[:, 0:1], None,
                            ALU.is_equal).then_inc(onehot_ready, 1)
            link(v.scalar_tensor_tensor(same_before[:], idt[:, 2:2 + BATCH], idf[:, 0:1],
                                        const_of(C_BEFORE, BATCH, BATCH), ALU.is_equal, ALU.mult,
                                        accum_out=rank[:]))
            link(v.tensor_scalar(id1_wide[:], const_of(C_ONES, P, BATCH), idf[:, 1:2], None, ALU.mult))
            dve.wait_ge(counts_ready, 1)
            link(v.tensor_scalar(tiles_i[:], counts_ps[:], float(SLOTS - 1), None, ALU.add))
            link(v.tensor_scalar(tiles_s[:], tiles_i[:], SLOTS.bit_length() - 1, None, ALU.logical_shift_right))
            link(v.tensor_copy(tiles[:], tiles_s[:]))
            link(v.tensor_scalar(present[:], tiles[:], 1.0, None, ALU.min))
            link(v.tensor_tensor_scan(places_end[:], const_of(C_ONES, ADAPTERS), present[:], 0.0,
                                      ALU.mult, ALU.add))
            link(v.tensor_tensor(places[:], places_end[:], present[:], ALU.subtract))
            link(v.tensor_tensor(named[:], present[:], const_of(C_SLOT, ADAPTERS), ALU.mult))
            sq = [1, ADAPTERS, ADAPTERS]
            link(v.tensor_tensor(at_place[:],
                                 const_of(C_SLOT, ADAPTERS, 1).unsqueeze(2).broadcast_to(sq),
                                 places[0:1, :].unsqueeze(1).broadcast_to(sq), ALU.is_equal))
            link(v.tensor_tensor(at_place[:], at_place[:],
                                 named[0:1, :].unsqueeze(1).broadcast_to(sq), ALU.mult))
            with nc.allow_low_precision(reason="small whole numbers"):
                link(v.tensor_reduce(meta[:, M_USED:M_USED + ADAPTERS], at_place[:], AX.X, ALU.add))
            v.tensor_copy(meta[:, M_N_USED:M_N_USED + 1],
                          places_end[0:1, ADAPTERS - 1:ADAPTERS]).then_inc(used_ready, 1)
            link(v.tensor_tensor_scan(tiles_end[:], const_of(C_ONES, ADAPTERS), tiles[:], 0.0,
                                      ALU.mult, ALU.add))
            link(v.tensor_tensor(tiles_from[:], tiles_end[:], tiles[:], ALU.subtract))
            link(v.scalar_tensor_tensor(base_terms[:], tiles_from[0:BATCH, :], float(SLOTS), onehot[:],
                                        ALU.mult, ALU.mult, accum_out=base[:]))
            v.tensor_scalar(in_slot[:], const_of(C_SLOT, LISTED * SLOTS, BATCH), rank[:], base[:],
                            ALU.subtract, ALU.is_equal).then_inc(in_slot_ready, 1)
            dve.wait_ge(slots_ready, 1)
            full = [P, 2 * LISTED, SLOTS]
            link(v.tensor_tensor(picked[:], slots_ps[:].rearrange("p (t j) -> p t j", j=SLOTS),
                                 const_of(C_CHMASK, SLOTS).unsqueeze(1).broadcast_to(full), ALU.mult))
            link(v.tensor_reduce(picked_sum[:], picked[:], AX.X, ALU.add))
            link(v.tensor_scalar(x_index[:], picked_sum[:, 0:LISTED], const_of(C_XROW, 1), None, ALU.add))
            v.tensor_scalar(w1_index[:], picked_sum[:, LISTED:2 * LISTED], const_of(C_WROW, 1), None,
                            ALU.add).then_inc(index_ready, 1)
            link(v.tensor_scalar(last_tile[:], tiles_end[0:1, ADAPTERS - 1:ADAPTERS], -1.0, None, ALU.add))
            link(v.tensor_scalar(tile_no[:], const_of(C_SLOT, LISTED, 1), last_tile[:], None, ALU.min))
            wide = [1, LISTED, ADAPTERS]
            link(v.tensor_tensor(ended[:], tiles_end[0:1, :].unsqueeze(1).broadcast_to(wide),
                                 tile_no[:].unsqueeze(2).broadcast_to(wide), ALU.is_le))
            link(v.tensor_tensor(ended[:], ended[:], present[0:1, :].unsqueeze(1).broadcast_to(wide),
                                 ALU.mult))
            with nc.allow_low_precision(reason="small whole numbers"):
                link(v.tensor_reduce(meta[:, M_PLACE:M_PLACE + LISTED], ended[:], AX.X, ALU.add))
            link(v.tensor_scalar(half_i[:], tiles_end[0:1, ADAPTERS - 1:ADAPTERS], 1.0, None, ALU.add))
            v.tensor_scalar(meta[:, M_N_PAIRS:M_N_PAIRS + 1], half_i[:], 1, None,
                            ALU.logical_shift_right).then_inc(meta_ready, 1)

            def add_eye(k):
                dve.wait_ge(raw_landed[k % RAW_BUFS], 16 * (k // RAW_BUFS + 1))
                diag = w_raw[:, k % RAW_BUFS, :].rearrange("p (m c) -> p m c", c=P)[:, 0:CHUNKS * CHUNKS:CHUNKS + 1, :]
                v.tensor_tensor(diag, diag, const_of(C_IDENT, P).unsqueeze(1).broadcast_to([P, CHUNKS, P]),
                                ALU.add).then_inc(eye_added, 1)

            def weight_lo(k):
                dve.wait_ge(w_hi_ready, k + 1)
                v.tensor_tensor(w_lo[:, k, :], w_raw[:, k % RAW_BUFS, :], w_hi[:, k, :].bitcast(F32),
                                ALU.subtract).then_inc(w_split, 1)

            def diagonal(t, parity):
                dve.wait_ge(w1_landed[parity], 16 * (t // 2 + 1) if isinstance(t, int) else (t - parity) * 8 + 16)
                v.tensor_tensor(w1_eye[:, parity, :], w1_rows[:, parity, :], const_of(C_BLOCK, CH),
                                ALU.add).then_inc(w1_eye_ready, 1)
                dve.wait_ge(w1_eye_ready, t + 1)
                if not isinstance(t, int) or t >= 2:
                    dve.wait_ge(u_ready, t - 1)
                shape = [P, SLOTS, CH]
                v.tensor_tensor(block[:, parity, :].rearrange("p (j d) -> p j d", d=CH),
                                w1_eye[:, parity, :].unsqueeze(1).broadcast_to(shape),
                                const_of(C_MASK, SLOTS).unsqueeze(2).broadcast_to(shape),
                                ALU.mult).then_inc(block_ready, 1)

            def u_low(t, parity):
                dve.wait_ge(u_hi_ready, t + 1)
                if not isinstance(t, int) or t >= 2:
                    dve.wait_ge(z_ready, t - 1)
                v.tensor_tensor(u_lo[:, parity, :], u_ps[parity][:], u_hi[:, parity, :].bitcast(F32),
                                ALU.subtract).then_inc(u_split, 1)

            def half(t, parity, k=None):
                if k is None:
                    diagonal(t + 2, parity)
                    u_low(t + 1, 1 - parity)
                    return
                with dve.If(n_used > k):
                    add_eye(k)
                diagonal(t + 2, parity)
                u_low(t + 1, 1 - parity)
                with dve.If(n_used > k):
                    weight_lo(k)

            def pair(i, k=None):
                half(2 * i, 0, k)
                half(2 * i + 1, 1, None if k is None else k + 1)

            dve.wait_ge(meta_ready, 1)
            n_used = entry(dve, M_N_USED, ADAPTERS, 1)
            n_pairs = entry(dve, M_N_PAIRS, PAIRS, MIN_PAIRS)
            diagonal(0, 0)
            add_eye(0)
            diagonal(1, 1)
            weight_lo(0)
            u_low(0, 0)
            with dve.If(n_used > 1):
                add_eye(1)
                weight_lo(1)
            for i in range(SPLIT_PAIRS):
                pair(i, 2 * i + 2)
            with dve.Fori(SPLIT_PAIRS, MIN_PAIRS) as i:
                pair(i)
            optional_pairs(dve, n_pairs, pair)

        @prog.tensor
        def _(pe):
            pe.wait_ge(tables_landed, 32)
            pe.wait_ge(onehot_ready, 1)
            nc.tensor.matmul(counts_ps[:], const_of(C_ONES, P, BATCH), onehot[:]).then_inc(counts_ready, 1)
            pe.wait_ge(in_slot_ready, 1)
            n = LISTED * SLOTS
            nc.tensor.matmul(slots_ps[:, 0:n], const_of(C_BATCH, P, BATCH), in_slot[:])
            nc.tensor.matmul(slots_ps[:, n:2 * n], id1_wide[:], in_slot[:]).then_inc(slots_ready, 1)

            def stage1(t, parity):
                pe.wait_ge(x_landed[parity], 16 * (t // 2 + 1) if isinstance(t, int) else (t - parity) * 8 + 16)
                pe.wait_ge(block_ready, t + 1)
                if not isinstance(t, int) or t >= 2:
                    pe.wait_ge(u_split, t - 1)
                for c in range(CHUNKS):
                    last = nc.tensor.matmul(u_ps[parity][:, c * P:(c + 1) * P],
                                            x_tile[:, parity, c * P:(c + 1) * P], block[:, parity, :])
                last.then_inc(u_ready, 1)

            def stage2(t, parity):
                place = entry(pe, M_PLACE + t, ADAPTERS - 1)
                pe.wait_ge(u_split, t + 1)
                pe.wait_ge(w_split, place + 1)
                if not isinstance(t, int) or t >= 2:
                    pe.wait_ge(z_copied, t - 1)
                passes = [(u, w, c) for c in range(CHUNKS) for u, w in ((u_hi, w_hi), (u_hi, w_lo), (u_lo, w_hi))]
                for n, (u, w, c) in enumerate(passes):
                    last = nc.tensor.matmul(z_ps[parity][:], u[:, parity, c * P:(c + 1) * P],
                                            w[:, bass.ds(place, 1), c * STEPS:(c + 1) * STEPS],
                                            start=(n == 0), stop=(n == len(passes) - 1))
                last.then_inc(z_ready, 1)

            def pair(i):
                stage1(2 * i + 1, 1)
                stage2(2 * i, 0)
                stage1(2 * i + 2, 0)
                stage2(2 * i + 1, 1)

            pe.wait_ge(meta_ready, 1)
            n_pairs = entry(pe, M_N_PAIRS, PAIRS, MIN_PAIRS)
            stage1(0, 0)
            pair(0)
            with pe.Fori(1, MIN_PAIRS) as i:
                pair(i)
            optional_pairs(pe, n_pairs, pair)


def kernel(x, itok_B_3_7, itok_B_0_15, L0_cond_weight, L1_cond_weights):
    import concourse.bacc as bacc
    from concourse.bass_utils import run_bass_kernel_spmd

    x = np.ascontiguousarray(x)
    id0, id1 = np.asarray(itok_B_3_7), np.asarray(itok_B_0_15)
    ids = np.concatenate([id0[:, None], id1[:, None], np.broadcast_to(id0[None, :], (BATCH, BATCH))], axis=1)
    w0 = np.asarray(L0_cond_weight).transpose(0, 2, 1).reshape(ADAPTERS, CHUNKS, P, STEPS).transpose(0, 2, 1, 3)
    arrays = {
        "x": x.reshape(ROWS, STEPS),
        "ids": np.ascontiguousarray(ids),
        "w0": np.ascontiguousarray(w0).reshape(ADAPTERS, P, CHUNKS * STEPS),
        "w1": np.ascontiguousarray(np.asarray(L1_cond_weights).reshape(CONDS * CH, CH)),
        "const": constants(),
    }
    nc = bacc.Bacc("TRN2", target_bir_lowering=False, num_devices=1)
    args = {n: nc.dram_tensor(n, a.shape, mybir.dt.from_np(a.dtype), kind="ExternalInput").ap()
            for n, a in arrays.items()}
    out = nc.dram_tensor("out", (ROWS, STEPS), F32, kind="ExternalOutput").ap()
    build(nc, out=out, **args)
    done = run_bass_kernel_spmd(nc, [arrays], core_ids=[0])
    return done.results[0]["out"].reshape(BATCH, CH, STEPS)
```

```python
from contextlib import ExitStack

import concourse.bass as bass
import numpy as np
from concourse import mybir

F32 = mybir.dt.float32
BF16 = mybir.dt.bfloat16
F32R = mybir.dt.float32r
I32 = mybir.dt.int32
U32 = mybir.dt.uint32
ALU = mybir.AluOpType
AX = mybir.AxisListType

P = 128
BATCH, CH, STEPS = 64, 32, 512
ADAPTERS, CONDS = 8, 16
ROWS = BATCH * CH
SLOTS = P // CH
CHUNKS = STEPS // P
MIN_TILES = BATCH // SLOTS
MAX_TILES = (BATCH + ADAPTERS * (SLOTS - 1)) // SLOTS
GROUP = 4
LOOPS = (MIN_TILES - GROUP) // GROUP

C_SLOT = 0
C_BEFORE = C_SLOT + MAX_TILES * SLOTS
C_XROW = C_BEFORE + BATCH
C_WROW = C_XROW + 1
C_IDENT = C_WROW + 1
C_MASK = C_IDENT + P
C_BLOCK = C_MASK + SLOTS
C_END = C_BLOCK + CH

M_USED = 0
M_N_USED = M_USED + ADAPTERS
M_N_TILES = M_N_USED + 1
M_PLACE = M_N_TILES + 1
M_END = M_PLACE + MAX_TILES


def constants():
    c = np.zeros((P, C_END), np.float32)
    row = np.arange(P)
    c[:, C_SLOT:C_BEFORE] = np.arange(MAX_TILES * SLOTS)
    c[:, C_BEFORE:C_XROW] = np.arange(BATCH) < row[:, None]
    c[:, C_XROW] = ROWS + row % CH
    c[:, C_WROW] = row % CH
    c[:, C_IDENT:C_MASK] = np.eye(P)
    c[:, C_MASK:C_BLOCK] = row[:, None] // CH == np.arange(SLOTS)
    c[:, C_BLOCK:C_END] = row[:, None] % CH == np.arange(CH)
    return c


def build(nc, x, ids, w0, w1, const, out):
    with ExitStack() as ctx:
        def sb(name, shape, dt=F32):
            return ctx.enter_context(nc.sbuf_tensor(name, shape, dt))

        def sem(name):
            return ctx.enter_context(nc.semaphore(name))

        w_raw = sb("w_raw", [P, GROUP, CHUNKS * STEPS])
        w_hi = sb("w_hi", [P, ADAPTERS, CHUNKS * STEPS], F32R)
        w_lo = sb("w_lo", [P, ADAPTERS, CHUNKS * STEPS], F32R)
        x_tile = sb("x_tile", [P, GROUP, STEPS])
        w1_rows = sb("w1_rows", [P, GROUP, CH])
        w1_eye = sb("w1_eye", [P, 2, CH])
        block = sb("block", [P, 2, P])
        u_hi = sb("u_hi", [P, 2, CHUNKS * P], F32R)
        u_lo = sb("u_lo", [P, 2, CHUNKS * P], F32R)
        z_tile = sb("z_tile", [P, 2, STEPS])
        cst = sb("cst", [P, C_END])
        idt = sb("idt", [BATCH, 2 + BATCH], I32)
        ones = sb("ones", [BATCH, P], BF16)
        ones_row = sb("ones_row", [P, ADAPTERS])
        onehot = sb("onehot", [BATCH, ADAPTERS], BF16)
        below = sb("below", [BATCH, ADAPTERS])
        same_before = sb("same_before", [BATCH, BATCH])
        rank = sb("rank", [BATCH, 1])
        batch_at = sb("batch_at", [BATCH, SLOTS, P], BF16)
        cond_at = sb("cond_at", [BATCH, SLOTS, P], BF16)
        tiles = sb("tiles", [P, ADAPTERS], I32)
        tiles_end = sb("tiles_end", [1, ADAPTERS])
        present = sb("present", [1, ADAPTERS])
        places_end = sb("places_end", [1, ADAPTERS])
        named = sb("named", [1, ADAPTERS])
        at_place = sb("at_place", [1, ADAPTERS, ADAPTERS])
        base_terms = sb("base_terms", [BATCH, ADAPTERS])
        base = sb("base", [BATCH, 1])
        in_slot = sb("in_slot", [BATCH, MAX_TILES * SLOTS], BF16)
        x_index = sb("x_index", [P, MAX_TILES], U32)
        w1_index = sb("w1_index", [P, MAX_TILES], U32)
        last_tile = sb("last_tile", [1, 1])
        tile_no = sb("tile_no", [1, MAX_TILES])
        ended = sb("ended", [1, MAX_TILES, ADAPTERS])
        meta = sb("meta", [1, M_END], I32)

        counts_ps = ctx.enter_context(nc.psum_tensor("counts_ps", [P, ADAPTERS], F32))
        batch_ps = ctx.enter_context(nc.psum_tensor("batch_ps", [P, MAX_TILES], F32))
        cond_ps = ctx.enter_context(nc.psum_tensor("cond_ps", [P, MAX_TILES], F32))
        u_ps = [ctx.enter_context(nc.psum_tensor(f"u_ps{i}", [P, CHUNKS * P], F32)) for i in range(2)]
        z_ps = [ctx.enter_context(nc.psum_tensor(f"z_ps{i}", [P, STEPS], F32)) for i in range(2)]

        tables_landed = sem("tables_landed")
        rest_landed = sem("rest_landed")
        chunk_landed = [sem(f"chunk_landed{i}") for i in range(CHUNKS)]
        raw_landed = [sem(f"raw_landed{i}") for i in range(GROUP)]
        x_landed = [sem(f"x_landed{i}") for i in range(GROUP)]
        w1_landed = [sem(f"w1_landed{i}") for i in range(GROUP)]
        rows_asked = sem("rows_asked")
        rows_zeroed = sem("rows_zeroed")
        table_step = sem("table_step")
        onehot_ready = sem("onehot_ready")
        counts_ready = sem("counts_ready")
        in_slot_ready = sem("in_slot_ready")
        batch_ready = sem("batch_ready")
        cond_ready = sem("cond_ready")
        zeroed = sem("zeroed")
        cond_zeroed = sem("cond_zeroed")
        batch_at_ready = sem("batch_at_ready")
        cond_at_ready = sem("cond_at_ready")
        used_ready = sem("used_ready")
        index_ready = sem("index_ready")
        meta_ready = sem("meta_ready")
        eye_added = sem("eye_added")
        w_hi_ready = sem("w_hi_ready")
        w_split = sem("w_split")
        w1_eye_ready = sem("w1_eye_ready")
        block_ready = sem("block_ready")
        u_ready = sem("u_ready")
        u_hi_ready = sem("u_hi_ready")
        u_split = sem("u_split")
        z_ready = sem("z_ready")
        z_copied = sem("z_copied")
        z_stored = [sem(f"z_stored{i}") for i in range(2)]

        def const_of(start, width, rows=P):
            return cst[0:rows, start:start + width]

        def entry(eng, at, largest, least=0):
            return eng.value_load(meta[0:1, at:at + 1] if isinstance(at, int) else meta[0:1, bass.ds(at, 1)],
                                  min_val=least, max_val=largest)

        def split_count(k):
            return CHUNKS + k

        def hi_count(k, h):
            return CHUNKS + 2 * (k - 1) + h + 1

        def half_of(h):
            return slice(h * CHUNKS // 2 * STEPS, (h + 1) * CHUNKS // 2 * STEPS)

        def weight(parts, k, h):
            return parts[:, k, half_of(h)]

        def weight_after(g, r):
            return r + 1 if isinstance(g, int) else GROUP + r + 1

        def slot_rows(at):
            rows = at[:].rearrange("b j (i c) -> b (j i) c", c=CH)
            return rows[:, 0:SLOTS * SLOTS:SLOTS + 1, :]

        def known(g, r, least):
            return not isinstance(g, int) or GROUP * g + r >= least

        def pair_uses(g, r):
            return 2 * g + r // 2

        prog = ctx.enter_context(nc.Block())

        @prog.sync
        def _(sp):
            sp.dma_start(cst[:, 0:C_IDENT], const[:, 0:C_IDENT]).then_inc(tables_landed, 16)
            sp.dma_start(idt[:], ids).then_inc(tables_landed, 16)
            sp.dma_start(cst[:, C_IDENT:C_END], const[:, C_IDENT:C_END]).then_inc(rest_landed, 16)

            sp.wait_ge(used_ready, 1)
            which = entry(sp, M_USED, ADAPTERS - 1)
            for c in range(CHUNKS):
                sp.dma_start(w_raw[:, 0, c * STEPS:(c + 1) * STEPS],
                             w0[bass.ds(which, 1), :, c * STEPS:(c + 1) * STEPS].rearrange("a p n -> p (a n)")
                             ).then_inc(chunk_landed[c], 16)
            sp.wait_ge(meta_ready, 1)
            n_used = entry(sp, M_N_USED, ADAPTERS, 1)

            def load_from(k):
                with sp.If(n_used > k):
                    if k >= GROUP:
                        sp.wait_ge(w_split, split_count(k - GROUP))
                    sp.wait_ge(rows_asked, 2 if k == 1 else k + 2)
                    which = entry(sp, M_USED + k, ADAPTERS - 1)
                    sp.dma_start(w_raw[:, k % GROUP, :],
                                 w0[bass.ds(which, 1)].rearrange("a p n -> p (a n)")
                                 ).then_inc(raw_landed[k % GROUP], 16)
                    if k + 1 < ADAPTERS:
                        load_from(k + 1)
            load_from(1)

        @prog.gpsimd
        def _(pool):
            nc.gpsimd.memset(batch_at[:], 0.0).then_inc(zeroed, 1)
            nc.gpsimd.memset(ones[:], 1.0)
            pool.wait_ge(zeroed, 1)
            nc.gpsimd.iota(slot_rows(batch_at), pattern=[[0, SLOTS], [0, CH]], base=-BATCH,
                           channel_multiplier=1,
                           allow_small_or_imprecise_dtypes=True).then_inc(batch_at_ready, 1)
            nc.gpsimd.memset(x_tile[:], 0.0).then_inc(rows_zeroed, 1)
            pool.wait_ge(rows_zeroed, 1)

            def gather_x(t):
                if t >= GROUP:
                    pool.wait_ge(u_ready, t - GROUP + 1)
                nc.gpsimd.indirect_dma_start(
                    x_tile[:, t % GROUP, :], None, x,
                    bass.IndirectOffsetOnAxis(ap=x_index[:, t:t + 1], axis=0),
                    bounds_check=ROWS - 1, oob_is_err=False,
                    engine_sem=rows_asked).then_inc(x_landed[t % GROUP], 16)

            def gather_w1(t):
                if t >= GROUP:
                    pool.wait_ge(w1_eye_ready, t - GROUP + 1)
                nc.gpsimd.indirect_dma_start(
                    w1_rows[:, t % GROUP, :], None, w1,
                    bass.IndirectOffsetOnAxis(ap=w1_index[:, t:t + 1], axis=0),
                    bounds_check=CONDS * CH - 1, oob_is_err=False).then_inc(w1_landed[t % GROUP], 16)

            def scatter(t):
                pool.wait_ge(z_copied, t + 1)
                nc.gpsimd.indirect_dma_start(
                    out, bass.IndirectOffsetOnAxis(ap=x_index[:, t:t + 1], axis=0),
                    z_tile[:, t % 2, :], None,
                    bounds_check=ROWS - 1, oob_is_err=False).then_inc(z_stored[t % 2], 16)

            def step(t):
                gather_x(t + GROUP)
                gather_w1(t + GROUP)
                if t >= 1:
                    scatter(t - 1)

            def from_tile(t):
                def finish():
                    for last in range(t - 1, t + GROUP):
                        scatter(last)
                    for parity in range(2):
                        pool.wait_ge(z_stored[parity], 16 * ((t + GROUP + 1 - parity) // 2))

                if t + GROUP == MAX_TILES:
                    finish()
                    return
                with pool.If(n_tiles > t + GROUP):
                    step(t)
                    from_tile(t + 1)
                with pool.Else():
                    finish()

            pool.wait_ge(index_ready, 1)
            gather_x(0)
            pool.wait_ge(index_ready, 2)
            gather_w1(0)
            for t in range(1, GROUP):
                gather_x(t)
                gather_w1(t)
            for t in range(MIN_TILES - GROUP):
                step(t)
            pool.wait_ge(meta_ready, 1)
            n_tiles = entry(pool, M_N_TILES, MAX_TILES, MIN_TILES)
            from_tile(MIN_TILES - GROUP)

        @prog.scalar
        def _(act):
            act.wait_ge(cond_zeroed, 1)
            act.wait_ge(tables_landed, 32)
            nc.scalar.copy(slot_rows(cond_at),
                           idt[:, 1:2].unsqueeze(2).broadcast_to([BATCH, SLOTS, CH])).then_inc(cond_at_ready, 1)

            def weight_hi(k):
                act.wait_ge(eye_added, split_count(k))
                for h in range(2):
                    nc.scalar.copy(weight(w_hi, k, h), w_raw[:, k % GROUP, half_of(h)]).then_inc(w_hi_ready, 1)

            def u_high(g, r):
                act.wait_ge(u_ready, GROUP * g + r + 1)
                nc.scalar.copy(u_hi[:, r % 2, :], u_ps[r % 2][:]).then_inc(u_hi_ready, 1)

            def z_out(g, r):
                act.wait_ge(z_ready, GROUP * g + r + 1)
                if known(g, r, 2):
                    act.wait_ge(z_stored[r % 2], 16 * pair_uses(g, r))
                nc.scalar.copy(z_tile[:, r % 2, :], z_ps[r % 2][:]).then_inc(z_copied, 1)

            def step(g, r, weights=True):
                if known(g, r, 1):
                    z_out(g, r - 1)
                u_high(g, r + 1)
                if weights:
                    with act.If(n_used > GROUP * g + r + 1):
                        weight_hi(weight_after(g, r))

            def from_tile(t):
                def finish():
                    z_out(0, t - 1)
                    z_out(0, t)

                if t + 1 == MAX_TILES:
                    finish()
                    return
                with act.If(n_tiles > t + 1):
                    step(0, t, weights=False)
                    from_tile(t + 1)
                with act.Else():
                    finish()

            for c in range(CHUNKS):
                act.wait_ge(eye_added, c + 1)
                at = slice(c * STEPS, (c + 1) * STEPS)
                nc.scalar.copy(w_hi[:, 0, at], w_raw[:, 0, at]).then_inc(w_hi_ready, 1)
            u_high(0, 0)
            act.wait_ge(meta_ready, 1)
            n_used = entry(act, M_N_USED, ADAPTERS, 1)
            n_tiles = entry(act, M_N_TILES, MAX_TILES, MIN_TILES)
            for r in range(GROUP):
                step(0, r)
            with act.Fori(1, LOOPS) as g:
                for r in range(GROUP):
                    step(g, r, weights=GROUP + r + 1 < ADAPTERS)
            for t in range(GROUP * LOOPS, MIN_TILES - 1):
                step(0, t, weights=False)
            from_tile(MIN_TILES - 1)

        @prog.vector
        def _(dve):
            marked = [0]

            def mark(ins):
                marked[0] += 1
                ins.then_inc(table_step, 1)
                return marked[0]

            def after(step):
                dve.wait_ge(table_step, step)

            v = nc.vector
            v.memset(cond_at[:], 0.0).then_inc(cond_zeroed, 1)
            ones_set = mark(v.memset(ones_row[:], 1.0))
            dve.wait_ge(tables_landed, 32)
            adapter_no = const_of(C_SLOT, ADAPTERS, BATCH)
            v.tensor_scalar(onehot[:], adapter_no, idt[:, 0:1], None, ALU.is_equal).then_inc(onehot_ready, 1)
            mark(v.tensor_scalar(below[:], adapter_no, idt[:, 0:1], None, ALU.is_lt))
            ranked = mark(v.scalar_tensor_tensor(same_before[:], idt[:, 2:2 + BATCH], idt[:, 0:1],
                                                 const_of(C_BEFORE, BATCH, BATCH), ALU.is_equal, ALU.mult,
                                                 accum_out=rank[:]))
            dve.wait_ge(counts_ready, 1)
            tiled = mark(v.tensor_scalar(tiles[:], counts_ps[:], 1.0 / SLOTS, 0.5 - 0.5 / SLOTS,
                                         ALU.mult, ALU.add))
            seen = mark(v.tensor_scalar(present[:], counts_ps[0:1, :], 0.0, None, ALU.is_gt))
            after(tiled)
            based = mark(v.scalar_tensor_tensor(base_terms[:], tiles[0:BATCH, :], float(SLOTS), below[:],
                                                ALU.mult, ALU.mult, accum_out=base[:]))
            after(seen)
            placed = mark(v.tensor_tensor_scan(places_end[:], ones_row[0:1, :], present[:], 0.0,
                                               ALU.mult, ALU.add))
            after(based)
            v.tensor_scalar(in_slot[:], const_of(C_SLOT, MAX_TILES * SLOTS, BATCH), rank[:], base[:],
                            ALU.subtract, ALU.is_equal).then_inc(in_slot_ready, 1)
            naming = mark(v.tensor_tensor(named[:], present[:], const_of(C_SLOT, ADAPTERS, 1), ALU.mult))
            sq = [1, ADAPTERS, ADAPTERS]
            after(placed)
            matched = mark(v.tensor_tensor(at_place[:],
                                           const_of(C_SLOT + 1, ADAPTERS, 1).unsqueeze(2).broadcast_to(sq),
                                           places_end[:].unsqueeze(1).broadcast_to(sq), ALU.is_equal))
            tiled_to = mark(v.tensor_tensor_scan(tiles_end[:], ones_row[0:1, :], tiles[0:1, :], 0.0,
                                                 ALU.mult, ALU.add))
            after(matched)
            matched = mark(v.tensor_tensor(at_place[:], at_place[:],
                                           named[:].unsqueeze(1).broadcast_to(sq), ALU.mult))
            dve.wait_ge(batch_ready, 1)
            v.tensor_scalar(x_index[:], batch_ps[:], float(CH), const_of(C_XROW, 1), ALU.mult,
                            ALU.add).then_inc(index_ready, 1)
            after(matched)
            with nc.allow_low_precision(reason="small whole numbers"):
                v.tensor_reduce(meta[:, M_USED:M_USED + ADAPTERS], at_place[:], AX.X,
                                ALU.add).then_inc(used_ready, 1)
            dve.wait_ge(cond_ready, 1)
            v.tensor_scalar(w1_index[:], cond_ps[:], float(CH), const_of(C_WROW, 1), ALU.mult,
                            ALU.add).then_inc(index_ready, 1)
            after(tiled_to)
            lasting = mark(v.tensor_scalar(last_tile[:], tiles_end[:, ADAPTERS - 1:ADAPTERS], -1.0, None,
                                           ALU.add))
            mark(v.tensor_copy(meta[:, M_N_TILES:M_N_TILES + 1], tiles_end[:, ADAPTERS - 1:ADAPTERS]))
            mark(v.tensor_copy(meta[:, M_N_USED:M_N_USED + 1], places_end[:, ADAPTERS - 1:ADAPTERS]))
            after(lasting)
            after(mark(v.tensor_scalar(tile_no[:], const_of(C_SLOT, MAX_TILES, 1), last_tile[:], None, ALU.min)))
            wide = [1, MAX_TILES, ADAPTERS]
            after(mark(v.tensor_tensor(ended[:], tiles_end[:].unsqueeze(1).broadcast_to(wide),
                                       tile_no[:].unsqueeze(2).broadcast_to(wide), ALU.is_le)))
            after(mark(v.tensor_tensor(ended[:], ended[:], present[:].unsqueeze(1).broadcast_to(wide),
                                       ALU.mult)))
            with nc.allow_low_precision(reason="small whole numbers"):
                v.tensor_reduce(meta[:, M_PLACE:M_PLACE + MAX_TILES], ended[:], AX.X,
                                ALU.add).then_inc(meta_ready, 1)

            def diag_blocks(buf, chunks):
                blocks = w_raw[:, buf, :].rearrange("p (m c) -> p m c", c=P)
                return blocks[:, chunks.start * (CHUNKS + 1):(chunks.stop - 1) * (CHUNKS + 1) + 1:CHUNKS + 1, :]

            def add_eye(buf, chunks=range(CHUNKS)):
                diag = diag_blocks(buf, chunks)
                v.tensor_tensor(diag, diag, const_of(C_IDENT, P).unsqueeze(1).broadcast_to([P, len(chunks), P]),
                                ALU.add).then_inc(eye_added, 1)

            def weight_eye(k):
                uses = k // GROUP if k % GROUP == 0 else k // GROUP + 1
                dve.wait_ge(raw_landed[k % GROUP], 16 * uses)
                add_eye(k % GROUP)

            def weight_lo(k):
                for h in range(2):
                    dve.wait_ge(w_hi_ready, hi_count(k, h))
                    last = v.tensor_tensor(weight(w_lo, k, h), w_raw[:, k % GROUP, half_of(h)],
                                           weight(w_hi, k, h).bitcast(F32), ALU.subtract)
                last.then_inc(w_split, 1)

            def chunk_lo(c):
                dve.wait_ge(w_hi_ready, c + 1)
                at = slice(c * STEPS, (c + 1) * STEPS)
                v.tensor_tensor(w_lo[:, 0, at], w_raw[:, 0, at], w_hi[:, 0, at].bitcast(F32),
                                ALU.subtract).then_inc(w_split, 1)

            def diagonal(g, r):
                t, buf = GROUP * g + r, r % GROUP
                dve.wait_ge(w1_landed[buf], 16 * (g + r // GROUP + 1))
                v.tensor_tensor(w1_eye[:, r % 2, :], w1_rows[:, buf, :], const_of(C_BLOCK, CH),
                                ALU.add).then_inc(w1_eye_ready, 1)
                dve.wait_ge(w1_eye_ready, t + 1)
                if known(g, r, 2):
                    dve.wait_ge(u_ready, t - 1)
                shape = [P, SLOTS, CH]
                v.tensor_tensor(block[:, r % 2, :].rearrange("p (j d) -> p j d", d=CH),
                                w1_eye[:, r % 2, :].unsqueeze(1).broadcast_to(shape),
                                const_of(C_MASK, SLOTS).unsqueeze(2).broadcast_to(shape),
                                ALU.mult).then_inc(block_ready, 1)

            def u_low(g, r):
                t = GROUP * g + r
                dve.wait_ge(u_hi_ready, t + 1)
                if known(g, r, 2):
                    dve.wait_ge(z_ready, t - 1)
                v.tensor_tensor(u_lo[:, r % 2, :], u_ps[r % 2][:], u_hi[:, r % 2, :].bitcast(F32),
                                ALU.subtract).then_inc(u_split, 1)

            def step(g, r, lo=True, eye=True):
                diagonal(g, r + 2)
                u_low(g, r + 1)
                if lo:
                    with dve.If(n_used > GROUP * g + r + 1):
                        weight_lo(weight_after(g, r))
                        if eye:
                            with dve.If(n_used > GROUP * g + r + 2):
                                weight_eye(weight_after(g, r) + 1)

            def from_tile(t):
                if t + 2 == MAX_TILES:
                    u_low(0, t + 1)
                    return
                with dve.If(n_tiles > t + 2):
                    step(0, t, lo=False)
                    from_tile(t + 1)
                with dve.Else():
                    u_low(0, t + 1)

            dve.wait_ge(rest_landed, 16)
            for c in range(CHUNKS):
                dve.wait_ge(chunk_landed[c], 16)
                add_eye(0, range(c, c + 1))
                if c == CHUNKS - 2:
                    diagonal(0, 0)
                if c >= 1:
                    chunk_lo(c - 1)
            chunk_lo(CHUNKS - 1)
            diagonal(0, 1)
            u_low(0, 0)
            dve.wait_ge(meta_ready, 1)
            n_used = entry(dve, M_N_USED, ADAPTERS, 1)
            n_tiles = entry(dve, M_N_TILES, MAX_TILES, MIN_TILES)
            with dve.If(n_used > 1):
                weight_eye(1)
            for r in range(GROUP):
                step(0, r)
            with dve.Fori(1, LOOPS) as g:
                for r in range(GROUP):
                    step(g, r, lo=GROUP + r + 1 < ADAPTERS, eye=GROUP + r + 2 < ADAPTERS)
            for t in range(GROUP * LOOPS, MIN_TILES - 2):
                step(0, t, lo=False)
            from_tile(MIN_TILES - 2)

        @prog.tensor
        def _(pe):
            pe.wait_ge(batch_at_ready, 1)
            pe.wait_ge(onehot_ready, 1)
            nc.tensor.matmul(counts_ps[:], ones[:], onehot[:]).then_inc(counts_ready, 1)
            pe.wait_ge(in_slot_ready, 1)
            slot_of = in_slot[:].rearrange("b (t j) -> b j t", j=SLOTS)
            for j in range(SLOTS):
                last = nc.tensor.matmul(batch_ps[:], batch_at[:, j, :], slot_of[:, j, :],
                                        start=(j == 0), stop=(j == SLOTS - 1))
            last.then_inc(batch_ready, 1)
            pe.wait_ge(cond_at_ready, 1)
            for j in range(SLOTS):
                last = nc.tensor.matmul(cond_ps[:], cond_at[:, j, :], slot_of[:, j, :],
                                        start=(j == 0), stop=(j == SLOTS - 1))
            last.then_inc(cond_ready, 1)

            def stage1(g, r):
                t, buf = GROUP * g + r, r % GROUP
                pe.wait_ge(x_landed[buf], 16 * (g + r // GROUP + 1))
                pe.wait_ge(block_ready, t + 1)
                if known(g, r, 2):
                    pe.wait_ge(u_split, t - 1)
                for c in range(CHUNKS):
                    last = nc.tensor.matmul(u_ps[r % 2][:, c * P:(c + 1) * P],
                                            x_tile[:, buf, c * P:(c + 1) * P], block[:, r % 2, :])
                last.then_inc(u_ready, 1)

            def stage2(g, r):
                t = GROUP * g + r
                first = isinstance(g, int) and t == 0
                if not first:
                    place = entry(pe, M_PLACE + t, ADAPTERS - 1)
                pe.wait_ge(u_split, t + 1)
                if not first:
                    pe.wait_ge(w_split, place + CHUNKS)
                if known(g, r, 2):
                    pe.wait_ge(z_copied, t - 1)
                for c in range(CHUNKS):
                    if first:
                        pe.wait_ge(w_split, c + 1)
                    for n, (u, w) in enumerate(((u_hi, w_hi), (u_hi, w_lo), (u_lo, w_hi))):
                        at = slice(c * STEPS, (c + 1) * STEPS)
                        last = nc.tensor.matmul(z_ps[r % 2][:], u[:, r % 2, c * P:(c + 1) * P],
                                                w[:, 0, at] if first else w[:, bass.ds(place, 1), at],
                                                start=(c == 0 and n == 0), stop=(c == CHUNKS - 1 and n == 2))
                last.then_inc(z_ready, 1)

            def step(g, r):
                stage1(g, r + 1)
                stage2(g, r)

            def from_tile(t):
                if t + 1 == MAX_TILES:
                    stage2(0, t)
                    return
                with pe.If(n_tiles > t + 1):
                    step(0, t)
                    from_tile(t + 1)
                with pe.Else():
                    stage2(0, t)

            stage1(0, 0)
            stage1(0, 1)
            stage2(0, 0)
            pe.wait_ge(meta_ready, 1)
            n_tiles = entry(pe, M_N_TILES, MAX_TILES, MIN_TILES)
            for r in range(1, GROUP):
                step(0, r)
            with pe.Fori(1, LOOPS) as g:
                for r in range(GROUP):
                    step(g, r)
            for t in range(GROUP * LOOPS, MIN_TILES - 1):
                step(0, t)
            from_tile(MIN_TILES - 1)


def kernel(x, itok_B_3_7, itok_B_0_15, L0_cond_weight, L1_cond_weights):
    import concourse.bacc as bacc
    from concourse.bass_utils import run_bass_kernel_spmd

    x = np.ascontiguousarray(x)
    id0, id1 = np.asarray(itok_B_3_7), np.asarray(itok_B_0_15)
    ids = np.concatenate([id0[:, None], id1[:, None], np.broadcast_to(id0[None, :], (BATCH, BATCH))], axis=1)
    w0 = np.asarray(L0_cond_weight).transpose(0, 2, 1).reshape(ADAPTERS, CHUNKS, P, STEPS).transpose(0, 2, 1, 3)
    arrays = {
        "x": x.reshape(ROWS, STEPS),
        "ids": np.ascontiguousarray(ids),
        "w0": np.ascontiguousarray(w0).reshape(ADAPTERS, P, CHUNKS * STEPS),
        "w1": np.ascontiguousarray(np.asarray(L1_cond_weights).reshape(CONDS * CH, CH)),
        "const": constants(),
    }
    nc = bacc.Bacc("TRN2", target_bir_lowering=False, num_devices=1)
    args = {n: nc.dram_tensor(n, a.shape, mybir.dt.from_np(a.dtype), kind="ExternalInput").ap()
            for n, a in arrays.items()}
    out = nc.dram_tensor("out", (ROWS, STEPS), F32, kind="ExternalOutput").ap()
    build(nc, out=out, **args)
    done = run_bass_kernel_spmd(nc, [arrays], core_ids=[0])
    return done.results[0]["out"].reshape(BATCH, CH, STEPS)
```

```python
from contextlib import ExitStack

import concourse.bass as bass
import numpy as np
from concourse import mybir

F32 = mybir.dt.float32
BF16 = mybir.dt.bfloat16
F32R = mybir.dt.float32r
I32 = mybir.dt.int32
U32 = mybir.dt.uint32
ALU = mybir.AluOpType
AX = mybir.AxisListType

P = 128
BATCH, CH, STEPS = 64, 32, 512
ADAPTERS, CONDS = 8, 16
ROWS = BATCH * CH
SLOTS = P // CH
CHUNKS = STEPS // P
MIN_TILES = BATCH // SLOTS
MAX_TILES = (BATCH + ADAPTERS * (SLOTS - 1)) // SLOTS
GROUP = 4
WARM_UP = 14
LOOPS = (MIN_TILES - GROUP) // GROUP

C_SLOT = 0
C_BEFORE = C_SLOT + MAX_TILES * SLOTS
C_XROW = C_BEFORE + BATCH
C_WROW = C_XROW + 1
C_IDENT = C_WROW + 1
C_MASK = C_IDENT + P
C_BLOCK = C_MASK + SLOTS
C_END = C_BLOCK + CH
I_ADAPTER, I_COND, I_ALL = C_IDENT, C_IDENT + 1, C_IDENT + 2
HEAD = I_ALL + BATCH

M_USED = 0
M_N_USED = M_USED + ADAPTERS
M_N_TILES = M_N_USED + 1
M_PLACE = M_N_TILES + 1
M_NEW = M_PLACE + MAX_TILES
M_END = M_NEW + MAX_TILES


def constants():
    c = np.zeros((P, C_END), np.float32)
    row = np.arange(P)
    c[:, C_SLOT:C_BEFORE] = np.arange(MAX_TILES * SLOTS)
    c[:, C_BEFORE:C_XROW] = np.arange(BATCH) < row[:, None]
    c[:, C_XROW] = ROWS + row % CH
    c[:, C_WROW] = row % CH
    c[:, C_IDENT:C_MASK] = np.eye(P)
    c[:, C_MASK:C_BLOCK] = row[:, None] // CH == np.arange(SLOTS)
    c[:, C_BLOCK:C_END] = row[:, None] % CH == np.arange(CH)
    return c


def build(nc, x, head, w0, w1, const, out):
    with ExitStack() as ctx:
        def sb(name, shape, dt=F32):
            return ctx.enter_context(nc.sbuf_tensor(name, shape, dt))

        def sem(name):
            return ctx.enter_context(nc.semaphore(name))

        w_raw = sb("w_raw", [P, GROUP, CHUNKS * STEPS])
        w_hi = sb("w_hi", [P, ADAPTERS, CHUNKS * STEPS], F32R)
        w_lo = sb("w_lo", [P, ADAPTERS, CHUNKS * STEPS], F32R)
        x_tile = sb("x_tile", [P, GROUP, STEPS])
        w1_rows = sb("w1_rows", [P, GROUP, CH])
        z_tile = sb("z_tile", [P, GROUP, STEPS])
        w1_eye = sb("w1_eye", [P, 2, CH])
        block = sb("block", [P, 2, P])
        u_hi = sb("u_hi", [P, 2, CHUNKS * P], F32R)
        u_lo = sb("u_lo", [P, 2, CHUNKS * P], F32R)
        head_sb = sb("head_sb", [P, HEAD], I32)
        const_sb = sb("const_sb", [P, C_END - C_IDENT])
        ones = sb("ones", [BATCH, P], BF16)
        zeros = sb("zeros", [P, STEPS], BF16)
        ones_row = sb("ones_row", [P, ADAPTERS])
        onehot = sb("onehot", [BATCH, ADAPTERS], BF16)
        below = sb("below", [BATCH, ADAPTERS])
        same_before = sb("same_before", [BATCH, BATCH])
        rank = sb("rank", [BATCH, 1])
        batch_at = sb("batch_at", [BATCH, SLOTS, P], BF16)
        cond_at = sb("cond_at", [BATCH, SLOTS, P], BF16)
        tiles = sb("tiles", [P, ADAPTERS], I32)
        tiles_end = sb("tiles_end", [1, ADAPTERS])
        present = sb("present", [1, ADAPTERS])
        places_end = sb("places_end", [1, ADAPTERS])
        named = sb("named", [1, ADAPTERS])
        at_place = sb("at_place", [1, ADAPTERS, ADAPTERS])
        base_terms = sb("base_terms", [BATCH, ADAPTERS])
        base = sb("base", [BATCH, 1])
        in_slot = sb("in_slot", [BATCH, MAX_TILES * SLOTS], BF16)
        x_index = sb("x_index", [P, MAX_TILES], U32)
        half_index = sb("half_index", [P, 2, MAX_TILES], U32)
        w1_index = sb("w1_index", [P, MAX_TILES], U32)
        last_tile = sb("last_tile", [1, 1])
        act_dummy = sb("act_dummy", [1, 1])
        tile_no = sb("tile_no", [1, MAX_TILES])
        ended = sb("ended", [1, MAX_TILES, ADAPTERS])
        later_place = sb("later_place", [1, MAX_TILES])
        meta = sb("meta", [1, M_END], I32)

        counts_ps = ctx.enter_context(nc.psum_tensor("counts_ps", [P, ADAPTERS], F32))
        batch_ps = ctx.enter_context(nc.psum_tensor("batch_ps", [P, MAX_TILES], F32))
        cond_ps = ctx.enter_context(nc.psum_tensor("cond_ps", [P, MAX_TILES], F32))
        u_last_ps = ctx.enter_context(nc.psum_tensor("u_last_ps", [P, CHUNKS // 2 * P], F32))
        u_ps = [ctx.enter_context(nc.psum_tensor(f"u_ps{i}", [P, CHUNKS * P], F32)) for i in range(2)]
        z_ps = [ctx.enter_context(nc.psum_tensor(f"z_ps{i}", [P, STEPS], F32)) for i in range(2)]

        head_landed = sem("head_landed")
        rest_landed = sem("rest_landed")
        chunk_landed = [sem(f"chunk_landed{i}") for i in range(CHUNKS)]
        weight_landed = [sem(f"weight_landed{i}") for i in range(ADAPTERS)]
        weights_in = sem("weights_in")
        x_landed = [sem(f"x_landed{i}") for i in range(GROUP)]
        w1_landed = [sem(f"w1_landed{i}") for i in range(GROUP)]
        rows_asked = sem("rows_asked")
        rows_zeroed = sem("rows_zeroed")
        table_step = sem("table_step")
        zeros_set = sem("zeros_set")
        onehot_ready = sem("onehot_ready")
        counts_ready = sem("counts_ready")
        in_slot_ready = sem("in_slot_ready")
        batch_ready = sem("batch_ready")
        cond_ready = sem("cond_ready")
        zeroed = sem("zeroed")
        cond_zeroed = sem("cond_zeroed")
        batch_at_ready = sem("batch_at_ready")
        cond_at_ready = sem("cond_at_ready")
        used_ready = sem("used_ready")
        index_ready = sem("index_ready")
        half_index_ready = sem("half_index_ready")
        meta_ready = sem("meta_ready")
        eye_added = sem("eye_added")
        w_hi_ready = sem("w_hi_ready")
        w_split = sem("w_split")
        w1_eye_ready = sem("w1_eye_ready")
        block_ready = sem("block_ready")
        u_ready = sem("u_ready")
        u_hi_ready = sem("u_hi_ready")
        u_split = sem("u_split")
        u_half_ready = sem("u_half_ready")
        u_hi_half_ready = sem("u_hi_half_ready")
        u_half_split = sem("u_half_split")
        z_ready = sem("z_ready")
        z_copied = sem("z_copied")
        z_stored = [sem(f"z_stored{i}") for i in range(GROUP)]

        def const_of(start, width, rows=P):
            if start < C_IDENT:
                return head_sb[0:rows, start:start + width].bitcast(F32)
            return const_sb[0:rows, start - C_IDENT:start - C_IDENT + width]

        def id_of(start, width=1):
            return head_sb[0:BATCH, start:start + width]

        def entry(eng, at, largest, least=0):
            return eng.value_load(meta[0:1, at:at + 1] if isinstance(at, int) else meta[0:1, bass.ds(at, 1)],
                                  min_val=least, max_val=largest)

        def chunk_of(parts, k, c):
            at = slice(c * STEPS, (c + 1) * STEPS)
            return parts[:, k, at] if isinstance(k, int) else parts[:, bass.ds(k, 1), at].squeeze(1)

        def chunk_count(k, c):
            return k * CHUNKS + (c + 1)

        def first_for(eng, g, r):
            return entry(eng, M_NEW + GROUP * g + r, ADAPTERS - 1)

        first_half, last_half = slice(0, CHUNKS // 2 * P), slice(CHUNKS // 2 * P, CHUNKS * P)

        def columns(h):
            return slice(h * STEPS // 2, (h + 1) * STEPS // 2)

        def slot_rows(at):
            rows = at[:].rearrange("b j (i c) -> b (j i) c", c=CH)
            return rows[:, 0:SLOTS * SLOTS:SLOTS + 1, :]

        def known(g, r, least):
            return not isinstance(g, int) or GROUP * g + r >= least

        prog = ctx.enter_context(nc.Block())

        @prog.sync
        def _(sp):
            sp.dma_start(head_sb[:], head).then_inc(head_landed, 16)
            sp.dma_start(const_sb[:], const).then_inc(rest_landed, 16)

            sp.wait_ge(used_ready, 1)
            which = entry(sp, M_USED, ADAPTERS - 1)
            for c in range(CHUNKS):
                sp.dma_start(chunk_of(w_raw, 0, c),
                             w0[bass.ds(which, 1), :, c * STEPS:(c + 1) * STEPS].rearrange("a p n -> p (a n)")
                             ).then_inc(chunk_landed[c], 16)
            sp.wait_ge(meta_ready, 1)
            n_used = entry(sp, M_N_USED, ADAPTERS, 1)

            def pass_on(k):
                sp.wait_ge(weight_landed[k], 32)
                sp.sem_inc(weights_in, 1)

            def load_from(k):
                with sp.If(n_used > k):
                    if k >= GROUP:
                        sp.wait_ge(w_split, chunk_count(k - GROUP, CHUNKS - 1))
                    which = entry(sp, M_USED + k, ADAPTERS - 1)
                    for h in range(2):
                        if k == 1 or h == 0:
                            sp.wait_ge(rows_asked, 2 + h if k == 1 else k + 2)
                        half = slice(h * CHUNKS // 2 * STEPS, (h + 1) * CHUNKS // 2 * STEPS)
                        sp.dma_start(w_raw[:, k % GROUP, half],
                                     w0[bass.ds(which, 1), :, half].rearrange("a p n -> p (a n)")
                                     ).then_inc(weight_landed[k], 16)
                    if k > 1:
                        pass_on(k - 1)
                    if k + 1 < ADAPTERS:
                        load_from(k + 1)
                    else:
                        pass_on(k)
                if k > 1:
                    with sp.Else():
                        pass_on(k - 1)
            load_from(1)

        @prog.gpsimd
        def _(pool):
            nc.gpsimd.memset(batch_at[:], 0.0).then_inc(zeroed, 1)
            nc.gpsimd.memset(ones[:], 1.0)
            pool.wait_ge(zeroed, 1)
            nc.gpsimd.iota(slot_rows(batch_at), pattern=[[0, SLOTS], [0, CH]], base=-BATCH,
                           channel_multiplier=1,
                           allow_small_or_imprecise_dtypes=True).then_inc(batch_at_ready, 1)
            nc.gpsimd.memset(x_tile[:], 0.0).then_inc(rows_zeroed, 1)
            pool.wait_ge(rows_zeroed, 1)

            def gather_x(t):
                if t >= GROUP:
                    pool.wait_ge(u_ready, t - GROUP + 1)
                nc.gpsimd.indirect_dma_start(
                    x_tile[:, t % GROUP, :], None, x,
                    bass.IndirectOffsetOnAxis(ap=x_index[:, t:t + 1], axis=0),
                    bounds_check=ROWS - 1, oob_is_err=False,
                    engine_sem=rows_asked).then_inc(x_landed[t % GROUP], 16)

            def gather_w1(t):
                if t >= GROUP:
                    pool.wait_ge(w1_eye_ready, t - GROUP + 1)
                nc.gpsimd.indirect_dma_start(
                    w1_rows[:, t % GROUP, :], None, w1,
                    bass.IndirectOffsetOnAxis(ap=w1_index[:, t:t + 1], axis=0),
                    bounds_check=CONDS * CH - 1, oob_is_err=False).then_inc(w1_landed[t % GROUP], 16)

            def scatter(t):
                pool.wait_ge(z_copied, t + 1)
                nc.gpsimd.indirect_dma_start(
                    out, bass.IndirectOffsetOnAxis(ap=x_index[:, t:t + 1], axis=0),
                    z_tile[:, t % GROUP, :], None,
                    bounds_check=ROWS - 1, oob_is_err=False).then_inc(z_stored[t % GROUP], 16)

            def scatter_half(t, h):
                pool.wait_ge(z_copied, t + 1 + h)
                nc.gpsimd.indirect_dma_start(
                    out.rearrange("r (h s) -> (r h) s", h=2),
                    bass.IndirectOffsetOnAxis(ap=half_index[:, h, t:t + 1], axis=0),
                    z_tile[:, t % GROUP, columns(h)], None,
                    bounds_check=2 * ROWS - 1, oob_is_err=False).then_inc(z_stored[t % GROUP], 16)

            def step(t):
                gather_w1(t + GROUP)
                gather_x(t + GROUP)
                if t >= 1:
                    scatter(t - 1)

            def from_tile(t):
                def finish():
                    last = t + GROUP - 1
                    for late in range(t - 1, last):
                        scatter(late)
                    pool.wait_ge(half_index_ready, 1)
                    for h in range(2):
                        scatter_half(last, h)
                    for buf in range(GROUP):
                        pool.wait_ge(z_stored[buf], 16 * ((last + GROUP - buf) // GROUP + (buf == last % GROUP)))

                if t + GROUP == MAX_TILES:
                    finish()
                    return
                with pool.If(n_tiles > t + GROUP):
                    step(t)
                    from_tile(t + 1)
                with pool.Else():
                    finish()

            pool.wait_ge(index_ready, 1)
            gather_w1(0)
            pool.wait_ge(index_ready, 2)
            gather_x(0)
            for t in range(1, GROUP):
                gather_w1(t)
                gather_x(t)
            for t in range(MIN_TILES - GROUP):
                step(t)
            pool.wait_ge(meta_ready, 1)
            n_tiles = entry(pool, M_N_TILES, MAX_TILES, MIN_TILES)
            from_tile(MIN_TILES - GROUP)

        @prog.scalar
        def _(act):
            act.wait_ge(zeros_set, 1)
            nc.scalar.copy(act_dummy[:], zeros[0:1, 0:1])
            act.wait_ge(cond_zeroed, 1)
            act.wait_ge(head_landed, 16)
            nc.scalar.copy(slot_rows(cond_at),
                           id_of(I_COND).unsqueeze(2).broadcast_to([BATCH, SLOTS, CH])).then_inc(cond_at_ready, 1)

            def chunk_hi(k, c):
                nc.scalar.copy(chunk_of(w_hi, k, c), chunk_of(w_raw, k % GROUP, c)).then_inc(w_hi_ready, 1)

            def hi_of(k):
                with act.If(k > 0):
                    act.wait_ge(eye_added, k + CHUNKS)
                    for c in range(CHUNKS):
                        chunk_hi(k, c)

            def u_high(g, r):
                act.wait_ge(u_ready, GROUP * g + r + 1)
                nc.scalar.copy(u_hi[:, r % 2, :], u_ps[r % 2][:]).then_inc(u_hi_ready, 1)

            def z_out(g, r):
                act.wait_ge(z_ready, GROUP * g + r + 1)
                buf = r % GROUP
                if known(g, r, GROUP):
                    act.wait_ge(z_stored[buf], 16 * (g + r // GROUP))
                nc.scalar.copy(z_tile[:, buf, :], z_ps[r % 2][:]).then_inc(z_copied, 1)

            def last_out(t):
                act.wait_ge(z_stored[t % GROUP], 16 * (t // GROUP))
                for h in range(2):
                    act.wait_ge(z_ready, t + 1 + h)
                    nc.scalar.copy(z_tile[:, t % GROUP, columns(h)],
                                   z_ps[(t + h) % 2][:, columns(h)]).then_inc(z_copied, 1)

            def step(g, r, k=None, ahead=True):
                if r + 2 < MAX_TILES and k is None:
                    k = first_for(act, g, r + 2)
                u_high(g, r + 1)
                if r + 2 < MAX_TILES:
                    hi_of(k)
                if ahead and r + 3 < MAX_TILES:
                    k = first_for(act, g, r + 3)
                z_out(g, r)
                return k

            def from_tile(t, k=None):
                if t + 1 == MAX_TILES:
                    last_out(t)
                    return
                with act.If(n_tiles > t + 1):
                    from_tile(t + 1, step(0, t, k))
                with act.Else():
                    last_out(t)

            act.wait_ge(meta_ready, 1)
            k1, k2 = first_for(act, 0, 1), first_for(act, 0, 2)
            for c in range(CHUNKS):
                if c == CHUNKS // 2:
                    act.wait_ge(u_half_ready, 1)
                    nc.scalar.copy(u_hi[:, 0, first_half], u_ps[0][:, first_half]).then_inc(u_hi_half_ready, 1)
                    act.wait_ge(u_ready, 1)
                    nc.scalar.copy(u_hi[:, 0, last_half], u_last_ps[:]).then_inc(u_hi_ready, 1)
                act.wait_ge(eye_added, c + 1)
                chunk_hi(0, c)
            hi_of(k1)
            k = step(0, 0, k2)
            for r in range(1, GROUP):
                k = step(0, r, k, ahead=r < GROUP - 1)
            n_tiles = entry(act, M_N_TILES, MAX_TILES, MIN_TILES)
            with act.Fori(1, LOOPS) as g:
                k = None
                for r in range(GROUP):
                    k = step(g, r, k, ahead=r < GROUP - 1)
            k = None
            for t in range(GROUP * LOOPS, MIN_TILES - 1):
                k = step(0, t, k)
            from_tile(MIN_TILES - 1, k)

        @prog.vector
        def _(dve):
            marked = [0]

            def mark(ins):
                marked[0] += 1
                ins.then_inc(table_step, 1)
                return marked[0]

            def after(step):
                dve.wait_ge(table_step, step)

            v = nc.vector
            v.memset(zeros[:], 0.0).then_inc(zeros_set, 1)
            v.memset(cond_at[:], 0.0).then_inc(cond_zeroed, 1)
            mark(v.memset(ones_row[:], 1.0))
            dve.wait_ge(head_landed, 16)
            adapter_no = const_of(C_SLOT, ADAPTERS, BATCH)
            v.tensor_scalar(onehot[:], adapter_no, id_of(I_ADAPTER), None, ALU.is_equal).then_inc(onehot_ready, 1)
            mark(v.tensor_scalar(below[:], adapter_no, id_of(I_ADAPTER), None, ALU.is_lt))
            mark(v.scalar_tensor_tensor(same_before[:], id_of(I_ALL, BATCH), id_of(I_ADAPTER),
                                                 const_of(C_BEFORE, BATCH, BATCH), ALU.is_equal, ALU.mult,
                                                 accum_out=rank[:]))
            dve.wait_ge(counts_ready, 1)
            tiled = mark(v.tensor_scalar(tiles[:], counts_ps[:], 1.0 / SLOTS, 0.5 - 0.5 / SLOTS,
                                         ALU.mult, ALU.add))
            seen = mark(v.tensor_scalar(present[:], counts_ps[0:1, :], 0.0, None, ALU.is_gt))
            after(tiled)
            based = mark(v.scalar_tensor_tensor(base_terms[:], tiles[0:BATCH, :], float(SLOTS), below[:],
                                                ALU.mult, ALU.mult, accum_out=base[:]))
            after(seen)
            placed = mark(v.tensor_tensor_scan(places_end[:], ones_row[0:1, :], present[:], 0.0,
                                               ALU.mult, ALU.add))
            after(based)
            v.tensor_scalar(in_slot[:], const_of(C_SLOT, MAX_TILES * SLOTS, BATCH), rank[:], base[:],
                            ALU.subtract, ALU.is_equal).then_inc(in_slot_ready, 1)
            mark(v.tensor_tensor(named[:], present[:], const_of(C_SLOT, ADAPTERS, 1), ALU.mult))
            sq = [1, ADAPTERS, ADAPTERS]
            after(placed)
            matched = mark(v.tensor_tensor(at_place[:],
                                           const_of(C_SLOT + 1, ADAPTERS, 1).unsqueeze(2).broadcast_to(sq),
                                           places_end[:].unsqueeze(1).broadcast_to(sq), ALU.is_equal))
            tiled_to = mark(v.tensor_tensor_scan(tiles_end[:], ones_row[0:1, :], tiles[0:1, :], 0.0,
                                                 ALU.mult, ALU.add))
            after(matched)
            matched = mark(v.tensor_tensor(at_place[:], at_place[:],
                                           named[:].unsqueeze(1).broadcast_to(sq), ALU.mult))
            dve.wait_ge(cond_ready, 1)
            v.tensor_scalar(w1_index[:], cond_ps[:], float(CH), const_of(C_WROW, 1), ALU.mult,
                            ALU.add).then_inc(index_ready, 1)
            dve.wait_ge(batch_ready, 1)
            v.tensor_scalar(x_index[:], batch_ps[:], float(CH), const_of(C_XROW, 1), ALU.mult,
                            ALU.add).then_inc(index_ready, 1)
            after(matched)
            with nc.allow_low_precision(reason="small whole numbers"):
                v.tensor_reduce(meta[:, M_USED:M_USED + ADAPTERS], at_place[:], AX.X,
                                ALU.add).then_inc(used_ready, 1)
            after(tiled_to)
            lasting = mark(v.tensor_scalar(last_tile[:], tiles_end[:, ADAPTERS - 1:ADAPTERS], -1.0, None,
                                           ALU.add))
            mark(v.tensor_copy(meta[:, M_N_TILES:M_N_TILES + 1], tiles_end[:, ADAPTERS - 1:ADAPTERS]))
            mark(v.tensor_copy(meta[:, M_N_USED:M_N_USED + 1], places_end[:, ADAPTERS - 1:ADAPTERS]))
            after(lasting)
            after(mark(v.tensor_scalar(tile_no[:], const_of(C_SLOT, MAX_TILES, 1), last_tile[:], None, ALU.min)))
            wide = [1, MAX_TILES, ADAPTERS]
            after(mark(v.tensor_tensor(ended[:], tiles_end[:].unsqueeze(1).broadcast_to(wide),
                                       tile_no[:].unsqueeze(2).broadcast_to(wide), ALU.is_le)))
            after(mark(v.tensor_tensor(ended[:], ended[:], present[:].unsqueeze(1).broadcast_to(wide),
                                       ALU.mult)))
            with nc.allow_low_precision(reason="small whole numbers"):
                counted = mark(v.tensor_reduce(meta[:, M_PLACE:M_PLACE + MAX_TILES], ended[:], AX.X, ALU.add))
            after(counted)
            place, new = (slice(m + 1, m + MAX_TILES) for m in (M_PLACE, M_NEW))
            after(mark(v.tensor_tensor(later_place[:, 1:], meta[:, place],
                                       meta[:, M_PLACE:M_PLACE + MAX_TILES - 1], ALU.is_gt)))
            v.tensor_tensor(meta[:, new], meta[:, place], later_place[:, 1:], ALU.mult).then_inc(meta_ready, 1)

            def add_eye(k, chunks=range(CHUNKS)):
                whole = w_raw[:, k, :] if isinstance(k, int) else w_raw[:, bass.ds(k % GROUP, 1), :].squeeze(1)
                blocks = whole.rearrange("p (m c) -> p m c", c=P)
                diag = blocks[:, chunks.start * (CHUNKS + 1):(chunks.stop - 1) * (CHUNKS + 1) + 1:CHUNKS + 1, :]
                v.tensor_tensor(diag, diag, const_of(C_IDENT, P).unsqueeze(1).broadcast_to([P, len(chunks), P]),
                                ALU.add).then_inc(eye_added, 1)

            def chunk_lo(k, c):
                dve.wait_ge(w_hi_ready, chunk_count(k, c))
                v.tensor_tensor(chunk_of(w_lo, k, c), chunk_of(w_raw, k % GROUP, c),
                                chunk_of(w_hi, k, c).bitcast(F32), ALU.subtract).then_inc(w_split, 1)

            def eye_of(k):
                with dve.If(k > 0):
                    dve.wait_ge(weights_in, k)
                    add_eye(k)

            def lo_of(k):
                with dve.If(k > 0):
                    for c in range(CHUNKS):
                        chunk_lo(k, c)

            def diagonal(g, r):
                t, buf = GROUP * g + r, r % GROUP
                dve.wait_ge(w1_landed[buf], 16 * (g + r // GROUP + 1))
                v.tensor_tensor(w1_eye[:, r % 2, :], w1_rows[:, buf, :], const_of(C_BLOCK, CH),
                                ALU.add).then_inc(w1_eye_ready, 1)
                dve.wait_ge(w1_eye_ready, t + 1)
                if known(g, r, 2):
                    dve.wait_ge(u_ready, t - 1)
                shape = [P, SLOTS, CH]
                v.tensor_tensor(block[:, r % 2, :].rearrange("p (j d) -> p j d", d=CH),
                                w1_eye[:, r % 2, :].unsqueeze(1).broadcast_to(shape),
                                const_of(C_MASK, SLOTS).unsqueeze(2).broadcast_to(shape),
                                ALU.mult).then_inc(block_ready, 1)

            def u_low(g, r):
                t = GROUP * g + r
                dve.wait_ge(u_hi_ready, t + 1)
                if known(g, r, 2):
                    dve.wait_ge(z_ready, t - 1)
                v.tensor_tensor(u_lo[:, r % 2, :], u_ps[r % 2][:], u_hi[:, r % 2, :].bitcast(F32),
                                ALU.subtract).then_inc(u_split, 1)

            def step(g, r, k2=None, k3=None):
                if k2 is None:
                    k2 = first_for(dve, g, r + 2)
                if k3 is None:
                    k3 = first_for(dve, g, r + 3)
                u_low(g, r + 1)
                diagonal(g, r + 3)
                if isinstance(g, int) and GROUP * g + r == 0:
                    eye_of(k2)
                lo_of(k2)
                eye_of(k3)
                return k3

            def from_tile(t):
                k2 = first_for(dve, 0, t + 2)

                def finish():
                    lo_of(k2)
                    with dve.If(n_tiles > t + 2):
                        u_low(0, t + 2)

                u_low(0, t + 1)
                if t + 3 == MAX_TILES:
                    finish()
                    return
                with dve.If(n_tiles > t + 3):
                    diagonal(0, t + 3)
                    lo_of(k2)
                    eye_of(first_for(dve, 0, t + 3))
                    from_tile(t + 1)
                with dve.Else():
                    finish()

            dve.wait_ge(index_ready, 2)
            dve.wait_ge(meta_ready, 1)
            k1, k2, k3 = (first_for(dve, 0, t) for t in (1, 2, 3))
            dve.wait_ge(rest_landed, 16)
            for c in range(CHUNKS):
                dve.wait_ge(chunk_landed[c], 16)
                add_eye(0, range(c, c + 1))
                if c == 1:
                    diagonal(0, 0)
                if 1 <= c < CHUNKS - 1:
                    chunk_lo(0, c - 1)
            for half, whole, high, split in ((first_half, u_ps[0][:, first_half], u_hi_half_ready, u_half_split),
                                             (last_half, u_last_ps[:], u_hi_ready, u_split)):
                dve.wait_ge(high, 1)
                v.tensor_tensor(u_lo[:, 0, half], whole, u_hi[:, 0, half].bitcast(F32),
                                ALU.subtract).then_inc(split, 1)
            diagonal(0, 1)
            chunk_lo(0, CHUNKS - 2)
            chunk_lo(0, CHUNKS - 1)
            diagonal(0, 2)
            for h in range(2):
                last = v.tensor_scalar(half_index[:, h, :], x_index[:], 2.0, float(h), ALU.mult, ALU.add)
            last.then_inc(half_index_ready, 1)
            eye_of(k1)
            lo_of(k1)
            k = step(0, 0, k2, k3)
            for r in range(1, GROUP):
                k = step(0, r, k)
            n_tiles = entry(dve, M_N_TILES, MAX_TILES, MIN_TILES)
            with dve.Fori(1, LOOPS) as g:
                k = None
                for r in range(GROUP):
                    k = step(g, r, k)
            for t in range(GROUP * LOOPS, MIN_TILES - 3):
                step(0, t)
            from_tile(MIN_TILES - 3)

        @prog.tensor
        def _(pe):
            pe.wait_ge(batch_at_ready, 1)
            pe.wait_ge(onehot_ready, 1)
            nc.tensor.matmul(counts_ps[:], ones[:], onehot[:]).then_inc(counts_ready, 1)
            pe.wait_ge(in_slot_ready, 1)
            slot_of = in_slot[:].rearrange("b (t j) -> b j t", j=SLOTS)

            def in_rows(result, values, ready):
                for j in range(SLOTS):
                    last = nc.tensor.matmul(result[:], values[:, j, :], slot_of[:, j, :],
                                            start=(j == 0), stop=(j == SLOTS - 1))
                last.then_inc(ready, 1)

            pe.wait_ge(cond_at_ready, 1)
            in_rows(cond_ps, cond_at, cond_ready)
            in_rows(batch_ps, batch_at, batch_ready)
            pe.wait_ge(zeros_set, 1)
            for _ in range(WARM_UP):
                nc.tensor.matmul(z_ps[0][:], zeros[:, 0:P], zeros[:])

            def stage1(g, r):
                t, buf = GROUP * g + r, r % GROUP
                pe.wait_ge(x_landed[buf], 16 * (g + r // GROUP + 1))
                pe.wait_ge(block_ready, t + 1)
                if known(g, r, 2):
                    pe.wait_ge(u_split, t - 1)
                for c in range(CHUNKS):
                    result = u_ps[r % 2][:, c * P:(c + 1) * P]
                    first = isinstance(g, int) and t == 0
                    if first and c >= CHUNKS // 2:
                        result = u_last_ps[:, (c - CHUNKS // 2) * P:(c - CHUNKS // 2 + 1) * P]
                    last = nc.tensor.matmul(result, x_tile[:, buf, c * P:(c + 1) * P], block[:, r % 2, :])
                    if first and c == CHUNKS // 2 - 1:
                        last.then_inc(u_half_ready, 1)
                last.then_inc(u_ready, 1)

            def stage2(g, r):
                t = GROUP * g + r
                first = isinstance(g, int) and t == 0
                if not first:
                    place = entry(pe, M_PLACE + t, ADAPTERS - 1)
                if first:
                    pe.wait_ge(u_hi_half_ready, 1)
                else:
                    pe.wait_ge(u_split, t + 1)
                    pe.wait_ge(w_split, chunk_count(place, CHUNKS - 1))
                if known(g, r, 2):
                    pe.wait_ge(z_copied, t - 1)
                for c in range(CHUNKS):
                    if first and c == CHUNKS // 2:
                        stage1(0, 1)
                        pe.wait_ge(u_split, 1)
                    if first:
                        pe.wait_ge(w_split, c + 1)
                    for n, (u, w) in enumerate(((u_hi, w_hi), (u_hi, w_lo), (u_lo, w_hi))):
                        at = slice(c * STEPS, (c + 1) * STEPS)
                        if first and c == 0 and u is u_lo:
                            pe.wait_ge(u_half_split, 1)
                        last = nc.tensor.matmul(z_ps[r % 2][:], u[:, r % 2, c * P:(c + 1) * P],
                                                w[:, 0, at] if first else w[:, bass.ds(place, 1), at],
                                                start=(c == 0 and n == 0), stop=(c == CHUNKS - 1 and n == 2))
                last.then_inc(z_ready, 1)

            def stage2_last(t):
                place = entry(pe, M_PLACE + t, ADAPTERS - 1)
                pe.wait_ge(u_split, t + 1)
                pe.wait_ge(w_split, chunk_count(place, CHUNKS - 1))
                for h in range(2):
                    pe.wait_ge(z_copied, t - 1 + h)
                    for c in range(CHUNKS):
                        at = slice(c * STEPS + h * STEPS // 2, c * STEPS + (h + 1) * STEPS // 2)
                        for n, (u, w) in enumerate(((u_hi, w_hi), (u_hi, w_lo), (u_lo, w_hi))):
                            last = nc.tensor.matmul(z_ps[(t + h) % 2][:, columns(h)],
                                                    u[:, t % 2, c * P:(c + 1) * P], w[:, bass.ds(place, 1), at],
                                                    start=(c == 0 and n == 0), stop=(c == CHUNKS - 1 and n == 2))
                    last.then_inc(z_ready, 1)

            def step(g, r):
                stage1(g, r + 1)
                stage2(g, r)

            def from_tile(t):
                if t + 1 == MAX_TILES:
                    stage2_last(t)
                    return
                with pe.If(n_tiles > t + 1):
                    step(0, t)
                    from_tile(t + 1)
                with pe.Else():
                    stage2_last(t)

            stage1(0, 0)
            stage2(0, 0)
            pe.wait_ge(meta_ready, 1)
            n_tiles = entry(pe, M_N_TILES, MAX_TILES, MIN_TILES)
            for r in range(1, GROUP):
                step(0, r)
            with pe.Fori(1, LOOPS) as g:
                for r in range(GROUP):
                    step(g, r)
            for t in range(GROUP * LOOPS, MIN_TILES - 1):
                step(0, t)
            from_tile(MIN_TILES - 1)


def kernel(x, itok_B_3_7, itok_B_0_15, L0_cond_weight, L1_cond_weights):
    import concourse.bacc as bacc
    from concourse.bass_utils import run_bass_kernel_spmd

    x = np.ascontiguousarray(x)
    id0, id1 = np.asarray(itok_B_3_7), np.asarray(itok_B_0_15)
    const = constants()
    head = np.zeros((P, HEAD), np.int32)
    head[:, :C_IDENT] = const[:, :C_IDENT].view(np.int32)
    head[:BATCH, I_ADAPTER], head[:BATCH, I_COND], head[:BATCH, I_ALL:] = id0, id1, id0
    w0 = np.asarray(L0_cond_weight).transpose(0, 2, 1).reshape(ADAPTERS, CHUNKS, P, STEPS).transpose(0, 2, 1, 3)
    arrays = {
        "x": x.reshape(ROWS, STEPS),
        "head": head,
        "w0": np.ascontiguousarray(w0).reshape(ADAPTERS, P, CHUNKS * STEPS),
        "w1": np.ascontiguousarray(np.asarray(L1_cond_weights).reshape(CONDS * CH, CH)),
        "const": np.ascontiguousarray(const[:, C_IDENT:]),
    }
    nc = bacc.Bacc("TRN2", target_bir_lowering=False, num_devices=1)
    args = {n: nc.dram_tensor(n, a.shape, mybir.dt.from_np(a.dtype), kind="ExternalInput").ap()
            for n, a in arrays.items()}
    out = nc.dram_tensor("out", (ROWS, STEPS), F32, kind="ExternalOutput").ap()
    build(nc, out=out, **args)
    done = run_bass_kernel_spmd(nc, [arrays], core_ids=[0])
    return done.results[0]["out"].reshape(BATCH, CH, STEPS)
```
